# Optimizing a Trainium2 kernel written in Bass

```python
import numpy as np
import jax
import jax.numpy as jnp

def _softmax(x, axis=-1):
    return jax.nn.softmax(x, axis=axis)
def _gelu(x):
    return jax.nn.gelu(x, approximate=True)
def _silu(x):
    return jax.nn.silu(x)
def _sigmoid(x):
    return jax.nn.sigmoid(x)
def _layernorm(x, axis=-1, eps=1e-5):
    m = jnp.mean(x, axis=axis, keepdims=True)
    v = jnp.var(x, axis=axis, keepdims=True)
    return (x - m) / jnp.sqrt(v + eps)
def _scatter_add(tgt, idx, src, axis=0):
    return tgt.at[idx].add(src)
def _segment_sum(src, seg, n):
    return jax.ops.segment_sum(src, seg, n)

kernel_name = 'mk_conv_seq_d1_conv_nhwc64_3acdc1'

def setup_inputs(seed: int = 0):
    np.random.seed(seed)
    _w = jnp.asarray
    def _rec_inputs():
        import jax
        import jax.numpy as jnp
        _gk = jax.random.key(seed)
        x = -0.000125 + 0.9999 * jax.random.normal(jax.random.fold_in(_gk, 1), (8, 128, 512, 64), jnp.float32)
        return x
    x = _rec_inputs()
    def _L0_conv_setup():
        import jax, jax.numpy as jnp
        import numpy as np
        B, C, N, T = (8, 128, 512, 64)
        key = jax.random.key(seed)
        ks = jax.random.split(key, 16)
        s = 0.05
        return {'x': jax.random.normal(ks[0], (B, C, N, T), jnp.float32), 'W_w': jax.random.normal(ks[1], (C, C), jnp.float32) * s, 'W_b': jax.random.normal(ks[2], (C,), jnp.float32) * s, 'conv_w': jax.random.normal(ks[3], (C, C), jnp.float32) * s, 'conv_b': jax.random.normal(ks[4], (C,), jnp.float32) * s, 'theta': jax.random.normal(ks[5], (C, C), jnp.float32) * s, 'memory': jax.random.normal(ks[6], (N, C), jnp.float32) * s, 'a_vec': jax.random.uniform(ks[7], (2 * C, 1), jnp.float32) * s, 'cw': jax.random.normal(ks[8], (N, N), jnp.float32) * s, 'cwa': jax.random.normal(ks[9], (N, N), jnp.float32) * s, 'fc_w': jax.random.normal(ks[10], (1, 2), jnp.float32) * s, 'fc_b': jax.random.normal(ks[11], (1,), jnp.float32) * s, 'emb': jax.random.normal(ks[12], (1, C, N, 1), jnp.float32), 'cheb': jax.random.normal(ks[13], (1, N, N), jnp.float32)}
    _L0_conv_all = _L0_conv_setup()
    _L0_conv_in = {k: v for k, v in _L0_conv_all.items() if k in ('W_w', 'W_b', 'conv_w', 'conv_b', 'theta', 'memory', 'a_vec', 'cw', 'cwa', 'fc_w', 'fc_b', 'emb', 'cheb', )}
    del _L0_conv_all

    return {
        "x": x,
        "L0_conv_W_w": _L0_conv_in["W_w"],
        "L0_conv_W_b": _L0_conv_in["W_b"],
        "L0_conv_conv_w": _L0_conv_in["conv_w"],
        "L0_conv_conv_b": _L0_conv_in["conv_b"],
        "L0_conv_theta": _L0_conv_in["theta"],
        "L0_conv_memory": _L0_conv_in["memory"],
        "L0_conv_a_vec": _L0_conv_in["a_vec"],
        "L0_conv_cw": _L0_conv_in["cw"],
        "L0_conv_cwa": _L0_conv_in["cwa"],
        "L0_conv_fc_w": _L0_conv_in["fc_w"],
        "L0_conv_fc_b": _L0_conv_in["fc_b"],
        "L0_conv_emb": _L0_conv_in["emb"],
        "L0_conv_cheb": _L0_conv_in["cheb"],
    }

def reference(x, L0_conv_W_w, L0_conv_W_b, L0_conv_conv_w, L0_conv_conv_b, L0_conv_theta, L0_conv_memory, L0_conv_a_vec, L0_conv_cw, L0_conv_cwa, L0_conv_fc_w, L0_conv_fc_b, L0_conv_emb, L0_conv_cheb):
    import jax
    import jax.numpy as jnp
    def _L0_conv_ref(x, W_w, W_b, conv_w, conv_b, theta, memory, a_vec, cw, cwa, fc_w, fc_b, emb, cheb):
        import jax, jax.numpy as jnp
        import numpy as np
        B, C, N, T = (8, 128, 512, 64)
        c = x.shape[1]
        skip = x
        xw = jnp.einsum('bcnt,dc->bdnt', x, W_w) + W_b[None, :, None, None]
        x_in = jnp.transpose(xw, (0, 3, 2, 1))
        h = x_in.sum(axis=1)
        Wh1 = h @ a_vec[:c]
        Wh2 = h @ a_vec[c:]
        e = Wh1 + jnp.transpose(Wh2, (0, 2, 1))
        adj_w = e * cw
        scale = 1.0 / jnp.sqrt(jnp.asarray(c, x.dtype))
        adj1 = jax.nn.softmax(jax.nn.relu(jnp.einsum('btnc,mc->bnm', x_in, memory) * scale), axis=-1)
        adj2 = jax.nn.softmax(jax.nn.relu(jnp.einsum('bnc,bmc->bnm', h, h) * scale), axis=-1)
        adj_f = jnp.stack([adj1, adj2], axis=-1) @ fc_w[0] + fc_b[0]
        adj_w = adj_w + adj_f * cwa
        adj_w = jax.nn.softmax(adj_w, axis=-1)
        n = adj_w.shape[-1]
        k = int(n * 0.8)
        _, idx = jax.lax.top_k(adj_w, k)
        bi = jnp.arange(adj_w.shape[0])[:, None, None]
        ni = jnp.arange(n)[None, :, None]
        mask = jnp.zeros_like(adj_w).at[bi, ni, idx].set(1.0)
        adj = adj_w * mask
        xh = jnp.einsum('bcnt,bnm->bcmt', xw, adj)
        xh = jnp.einsum('bcnt,cd->bdnt', xh, theta)
        out = jnp.einsum('bcnt,dc->bdnt', xh, conv_w) + conv_b[None, :, None, None]
        return out * emb + skip

    def _gn(v, G=32, eps=1e-5):
        B_, H_, W_, C_ = v.shape
        g = v.reshape(B_, H_, W_, G, C_ // G)
        m = jnp.mean(g, axis=(1, 2, 4), keepdims=True)
        s = jnp.var(g, axis=(1, 2, 4), keepdims=True)
        return ((g - m) / jnp.sqrt(s + eps)).reshape(v.shape)

    def _ln_c(v, eps=1e-6):
        m = jnp.mean(v, axis=-1, keepdims=True)
        s = jnp.var(v, axis=-1, keepdims=True)
        return (v - m) / jnp.sqrt(s + eps)

    def _ln_t(v, eps=1e-5):
        m = jnp.mean(v, axis=-1, keepdims=True)
        s = jnp.var(v, axis=-1, keepdims=True)
        return (v - m) / jnp.sqrt(s + eps)

    def _to_tokens(v):
        B_, H_, W_, C_ = v.shape
        return v.reshape(B_, H_ * W_, C_)
    def _from_tokens(t, like):
        return t.reshape(like.shape)

    x = _L0_conv_ref(x, L0_conv_W_w, L0_conv_W_b, L0_conv_conv_w, L0_conv_conv_b, L0_conv_theta, L0_conv_memory, L0_conv_a_vec, L0_conv_cw, L0_conv_cwa, L0_conv_fc_w, L0_conv_fc_b, L0_conv_emb, L0_conv_cheb)
    return x


_drawn_inputs = setup_inputs


def setup_inputs(seed=0):
    import zlib

    import numpy as np

    out = dict(_drawn_inputs(seed))
    spreads = {}
    factors = {'L0_conv_W_w': 7.439,
     'L0_conv_W_b': 4.09,
     'L0_conv_conv_w': 3.678,
     'L0_conv_theta': 3.4,
     'L0_conv_memory': 200.0,
     'L0_conv_a_vec': 8.0,
     'L0_conv_cw': 8.0,
     'L0_conv_cwa': 200.0,
     'L0_conv_fc_w': 200.0,
     'L0_conv_conv_b': 8.0}
    for name, (base, spread) in spreads.items():
        noise = np.random.default_rng([zlib.crc32(name.encode()), seed]).standard_normal(out[name].shape)
        drawn = base * np.exp(spread * noise) if base else spread * noise
        out[name] = jnp.asarray(drawn.astype(out[name].dtype))
    for name, factor in factors.items():
        out[name] = (out[name] * factor).astype(out[name].dtype)
    return out
```

```python
from contextlib import ExitStack

import numpy as np
import concourse.bass as bass
from concourse import mybir

F32 = mybir.dt.float32
F32R = mybir.dt.float32r
I32 = mybir.dt.int32
ALU = mybir.AluOpType
ACT = mybir.ActivationFunctionType
AX = mybir.AxisListType

B, C, N, T = 8, 128, 512, 64
P = 128
NT = N // P
KEEP = int(N * 0.8)
SCALE = float(np.float32(1.0) / np.sqrt(np.float32(C)))

BODY = 8
TURNS = T // BODY
LOOP_TURNS = 4
HALF = NT // 2
PAIRS = BODY // 2
POOL_PAIRS = 3
SPAN = PAIRS + POOL_PAIRS
POOL_ADDS = {0: 0, 1: 1, 2: 2, 4: 3, 5: 4, 6: 5}
SEARCHES = 6
BITS = (LOOP_TURNS + 1) * SEARCHES
SLOTS = BITS + SEARCHES
FIRST = BODY - SEARCHES
ENOUGH = 2 * KEEP - 1 - N

ZBUF = 4
BIG = 2.0 * N

CHMIX0, ZSUM0, ZL0, NODE0, SCALED0, ROW0, RELU0, SUMS0 = 2, 2, 1, 4, 2, 2, 1, 1
STEPS = 50


def build(nc, x, w_nat, w_t, w_b, theta_t, conv_t, conv_b, mem_t, a_vec, cw, cwa, fc, emb, bits_f, bits_i, cand0, out):
    with ExitStack() as ctx:
        def sb(name, shape, dt=F32):
            return ctx.enter_context(nc.sbuf_tensor(name, shape, dt))

        def ps(name, shape):
            return ctx.enter_context(nc.psum_tensor(name, shape, F32))

        def sem(name):
            return ctx.enter_context(nc.semaphore(name))

        x_in = sb("x_in", [P, PAIRS, 2, N])
        o_out = sb("o_out", [P, PAIRS, 2, N])
        stage_d = sb("stage_d", [P, PAIRS, 2, N])
        stage_p = sb("stage_p", [P, PAIRS, 2, N])
        xs_d = sb("xs_d", [P, N])
        xs_p = sb("xs_p", [P, N])
        adj_hi = sb("adj_hi", [P, NT, N], F32R)
        adj_lo = sb("adj_lo", [P, NT, N], F32R)
        prob = sb("prob", [P, NT, N])
        work = sb("work", [P, NT, 2, N])
        cw_sb = sb("cw_sb", [P, NT, N])
        cwa_sb = sb("cwa_sb", [P, NT, N])
        x_hi = sb("x_hi", [P, 2, N], F32R)
        x_lo = sb("x_lo", [P, 2, N], F32R)
        zsum = sb("zsum", [P, NT, P])
        z_hi = sb("z_hi", [P, ZBUF, NT, P], F32R)
        z_lo = sb("z_lo", [P, ZBUF, NT, P], F32R)
        scaled = sb("scaled", [P, 2, N])
        hT = sb("hT", [P, N])
        e_row = sb("e_row", [P, N])
        emb_sb = sb("emb_sb", [P, N])
        memT_sb = sb("memT_sb", [P, N])
        wT_sb = sb("wT_sb", [P, P])
        w_sb = sb("w_sb", [P, P])
        thT_sb = sb("thT_sb", [P, P])
        cvT_sb = sb("cvT_sb", [P, P])
        mixT = sb("mixT", [P, P])
        pT = sb("pT", [P, P])
        p_split = sb("p_split", [P, 2, P], F32R)
        pb_row = sb("pb_row", [P, P])
        wb_sb = sb("wb_sb", [P, 1])
        wb_t = sb("wb_t", [P, 1])
        cb_sb = sb("cb_sb", [P, 1])
        a_sb = sb("a_sb", [P, 2])
        fc_sb = sb("fc_sb", [P, 3])
        bitf_sb = sb("bitf_sb", [P, BITS + 1])
        biti_sb = sb("biti_sb", [P, BITS + 1], I32)
        cand0_sb = sb("cand0_sb", [P, NT], I32)
        cand = sb("cand", [P, NT], I32)
        miss = sb("miss", [P, NT], I32)
        count = sb("count", [P, NT])
        thr = sb("thr", [P, NT])
        kth = sb("kth", [P, NT])
        kth_neg = sb("kth_neg", [P, NT])
        balance = sb("balance", [P, NT])
        unequal = sb("unequal", [P, NT])
        ties_neg = sb("ties_neg", [P, NT])
        smax = sb("smax", [P, NT, 2])
        sneg = sb("sneg", [P, NT, 2])
        ssum = sb("ssum", [P, NT, 2])
        coef = sb("coef", [P, NT, 2])
        lmax = sb("lmax", [P, NT])
        lneg = sb("lneg", [P, NT])
        lsum = sb("lsum", [P, NT])
        lrec = sb("lrec", [P, NT])
        wh1 = sb("wh1", [P, NT])
        one = sb("one", [P, 1])
        sign = sb("sign", [P, NT, N])

        ps_mix = [ps(f"ps_mix{i}", [P, 2 * N]) for i in range(2)]
        ps_out = [ps(f"ps_out{i}", [P, N]) for i in range(2)]
        ps_adj = ps("ps_adj", [P, 2, N])

        consts_in = sem("consts_in")
        pair_in = [sem(f"pair_in{i}") for i in range(PAIRS)]
        pair_out = [sem(f"pair_out{i}") for i in range(PAIRS)]
        staged_d = [sem(f"staged_d{i}") for i in range(PAIRS)]
        staged_p = [sem(f"staged_p{i}") for i in range(PAIRS)]
        pre = sem("pre")
        pre_sb = sem("pre_sb")
        xh_ready = sem("xh_ready")
        xl_ready = sem("xl_ready")
        chmix_done = sem("chmix_done")
        zpart = sem("zpart")
        zsum_ready = sem("zsum_ready")
        zh_ready = sem("zh_ready")
        zl_ready = sem("zl_ready")
        node_done = sem("node_done")
        scaled_ready = sem("scaled_ready")
        row_done = sem("row_done")
        cleared_d = sem("cleared_d")
        cleared_p = sem("cleared_p")
        sums_d = sem("sums_d")
        sums_p = sem("sums_p")
        h_ps = sem("h_ps")
        h_sb = sem("h_sb")
        wh_ps = sem("wh_ps")
        erow_ready = sem("erow_ready")
        wh1_ready = sem("wh1_ready")
        s_done = sem("s_done")
        smax_ready = sem("smax_ready")
        relu_done = sem("relu_done")
        exp_done = sem("exp_done")
        attn_ready = sem("attn_ready")
        weighted = sem("weighted")
        logit_sum = sem("logit_sum")
        lneg_ready = sem("lneg_ready")
        lexp_done = sem("lexp_done")
        lrec_ready = sem("lrec_ready")
        prob_ready = sem("prob_ready")
        counted = sem("counted")
        missed = sem("missed")
        cand_ready = sem("cand_ready")
        kth_ready = sem("kth_ready")
        signed = sem("signed")
        balanced = sem("balanced")
        masked = sem("masked")
        ahi_ready = sem("ahi_ready")
        alo_dve = sem("alo_dve")
        alo_pool = sem("alo_pool")
        dve_step = sem("dve_step")

        N_CONST = 16 * 15
        MAKE_START = [0, 3, 6, 9]
        MASK_START = [0, 3, BODY, BODY + 3]
        PROJECT_H, PROJECT_WH = BODY + 2, BODY + 4

        def at(start, u, offset):
            return [i for i in range(NT) if start[i] + offset == u]

        def cands(k):
            return k + (1 if isinstance(k, int) and k < SEARCHES else 2)

        block = ctx.enter_context(nc.Block())

        @block.sync
        def _(sp):
            def load_x(g_pair, s):
                sp.dma_start(x_in[:, s, :, :], x_flat[g_pair]).then_inc(pair_in[s], 16)

            x_flat = x.rearrange("b q c k n -> (b q) c k n")
            o_flat = out.rearrange("b q c k n -> (b q) c k n")

            def stream_d(r, turn, s):
                sp.dma_start(stage_d[:, s, :, :], x[r, turn * SPAN + s]).then_inc(staged_d[s], 16)

            def stream_p(r, turn, s):
                sp.dma_start(stage_p[:, s, :, :], x[r, turn * SPAN + (PAIRS + s)]).then_inc(staged_p[s], 16)

            def stream_last(r, s):
                sp.dma_start(stage_p[:, s, :, :], x[r, LOOP_TURNS * SPAN + s]).then_inc(staged_p[s], 16)

            def summed(r, turn, s):
                sp.wait_ge(sums_d, r * (T // 2) + turn * BODY + (2 * s + 2 + SUMS0))
                sp.nop(nofuse=True)
                if s < POOL_PAIRS:
                    sp.wait_ge(sums_p, r * (T // 2) + turn * (2 * POOL_PAIRS) + (2 * s + 2 + SUMS0))
                sp.nop(nofuse=True)

            def next_stream(r, turn, s):
                summed(r, turn, s)
                stream_d(r, turn + 1, s)
                if s < POOL_PAIRS:
                    stream_p(r, turn + 1, s)

            def last_stream(r, s):
                if s < POOL_PAIRS:
                    summed(r, LOOP_TURNS - 1, s)
                stream_last(r, s)

            for s in range(PAIRS):
                stream_d(0, 0, s)
                if s < POOL_PAIRS:
                    stream_p(0, 0, s)
            for dst, src in ((w_sb, w_nat), (wT_sb, w_t), (thT_sb, theta_t), (cvT_sb, conv_t), (memT_sb, mem_t),
                             (emb_sb, emb), (wb_sb, w_b), (cb_sb, conv_b), (a_sb, a_vec), (bitf_sb, bits_f),
                             (biti_sb, bits_i), (cand0_sb, cand0)):
                sp.dma_start(dst[:, :], src).then_inc(consts_in, 16)
            sp.dma_start(fc_sb[:, :], fc.to_broadcast([P, 3])).then_inc(consts_in, 16)
            with sp.Fori(0, LOOP_TURNS - 1) as turn:
                for s in range(PAIRS):
                    next_stream(0, turn, s)
            for s in range(PAIRS):
                last_stream(0, s)
            for dst, src in ((cw_sb, cw), (cwa_sb, cwa)):
                sp.dma_start(dst[:, :, :], src.rearrange("(i p) m -> p i m", p=P)).then_inc(consts_in, 16)
            for s in range(PAIRS):
                load_x(s, s)

            def move(g_pair, s, last=False):
                sp.wait_ge(row_done, g_pair * 2 + (2 * s + 2 + ROW0))
                sp.dma_start(o_flat[g_pair + s], o_out[:, s, :, :]).then_inc(pair_out[s], 16)
                if not last:
                    load_x(g_pair + (PAIRS + s), s)

            def batch(b, main, sums, last=False):
                g_pair = b * (T // 2)
                r = b + 2
                if sums:
                    sp.wait_ge(sums_d, r * (T // 2) + SUMS0)
                    sp.nop(nofuse=True)
                    sp.wait_ge(sums_p, r * (T // 2) + SUMS0)
                    sp.nop(nofuse=True)
                    for s in range(PAIRS):
                        stream_d(r, 0, s)
                        if s < POOL_PAIRS:
                            stream_p(r, 0, s)
                if main:
                    for k in range(2):
                        for s in range(PAIRS):
                            move(g_pair + k * PAIRS, s)
                if sums or main:
                    with sp.Fori(0, LOOP_TURNS - 1) as turn:
                        for s in range(PAIRS):
                            if main:
                                move(g_pair + turn * PAIRS + 2 * PAIRS, s)
                            if sums:
                                next_stream(r, turn, s)
                for k in (5, 6, 7):
                    for s in range(PAIRS):
                        if main:
                            move(g_pair + k * PAIRS, s, last and k == 7)
                        if sums and k == 5:
                            last_stream(r, s)

            batch(-1, False, True)
            with sp.Fori(0, B - 2) as b:
                batch(b, True, True)
            batch(B - 2, True, False)
            batch(B - 1, True, False, last=True)
            for s in range(PAIRS):
                sp.wait_ge(pair_out[s], 16 * (B * TURNS + 1))

        @block.tensor
        def _(pe):
            pe.sem_inc(chmix_done, CHMIX0)
            pe.sem_inc(node_done, NODE0)
            pe.wait_ge(consts_in, N_CONST)
            nc.tensor.matmul(ps_adj[:, 0, 0:P], thT_sb[:, :], cvT_sb[:, :], start=True, stop=True).then_inc(pre, 1)
            pe.wait_ge(pre_sb, 1)
            nc.tensor.matmul(ps_adj[:, 1, 0:P], w_sb[:, :], mixT[:, :], start=True, stop=True).then_inc(pre, 1)
            pe.wait_ge(pre_sb, 2)
            nc.tensor.matmul(ps_adj[:, 0, 0:P], wb_sb[:, 0:1].to_broadcast([P, P]), mixT[:, :], start=True, stop=True).then_inc(pre, 1)
            pe.wait_ge(pre_sb, 5)

            def project_h(r):
                pe.wait_ge(sums_d, r * (T // 2) + (T // 2 + SUMS0))
                pe.wait_ge(sums_p, r * (T // 2) + (T // 2 + SUMS0))
                pe.wait_ge(relu_done, r * NT + RELU0)
                nc.tensor.matmul(ps_adj[:, 0, :], wT_sb[:, :], xs_d[:, :], start=True, stop=False)
                nc.tensor.matmul(ps_adj[:, 0, :], wT_sb[:, :], xs_p[:, :], start=False, stop=True).then_inc(h_ps, 1)

            def project_wh(r):
                pe.wait_ge(h_sb, r + 1)
                nc.tensor.matmul(ps_adj[:, 1, :], a_sb[:, 1:2].to_broadcast([P, P]), hT[:, :], start=True, stop=True)
                for i in range(NT):
                    last = nc.tensor.matmul(ps_adj[:, 0, i:i + 1], hT[:, i * P:(i + 1) * P], a_sb[:, 0:1], start=True, stop=True)
                last.then_inc(wh_ps, 1)

            def scores(a, i):
                if i == 0:
                    pe.wait_ge(erow_ready, a + 1)
                    pe.wait_ge(wh1_ready, a + 1)
                else:
                    pe.wait_ge(relu_done, a * NT + i + RELU0)
                h_i = hT[:, i * P:(i + 1) * P]
                nc.tensor.matmul(ps_adj[:, 0, :], h_i, memT_sb[:, :], start=True, stop=True)
                nc.tensor.matmul(ps_adj[:, 1, :], h_i, hT[:, :], start=True, stop=True).then_inc(s_done, 1)

            def make(a, u):
                for i in at(MAKE_START, u, 0):
                    scores(a, i)

            def project(r, u):
                if u == PROJECT_H:
                    project_h(r)
                if u == PROJECT_WH:
                    project_wh(r)

            def channel_mix(g, u):
                pe.wait_ge(xl_ready, g + (u + 1))
                pe.wait_ge(zsum_ready, g + (u - 1 + ZSUM0))
                o = ps_mix[u % 2]
                for i in range(NT):
                    c = i * 2 * P
                    nc.tensor.matmul(o[:, c:c + 2 * P], x_hi[:, u % 2, i * P:(i + 1) * P], p_split[:, :, :].rearrange("p s d -> p (s d)"), start=True, stop=False)
                    last = nc.tensor.matmul(o[:, c:c + P], x_lo[:, u % 2, i * P:(i + 1) * P], p_split[:, 0, :], start=False, stop=True)
                last.then_inc(chmix_done, 1)

            def node_mix(b, g, u, first=False):
                pe.wait_ge(zl_ready, g + (u + 1 + ZL0))
                pe.wait_ge(scaled_ready, g + (u - 1 + SCALED0))
                o = ps_out[u % 2][:, :]
                for i in range(NT):
                    if first:
                        if i < NT - 1:
                            pe.wait_ge(alo_dve, b * (NT - 1) + (i + 1))
                        else:
                            pe.wait_ge(alo_pool, b + 1)
                    nc.tensor.matmul(o, z_hi[:, u % ZBUF, i, :], adj_hi[:, i, :], start=i == 0, stop=False)
                    nc.tensor.matmul(o, z_hi[:, u % ZBUF, i, :], adj_lo[:, i, :], start=False, stop=False)
                    last = nc.tensor.matmul(o, z_lo[:, u % ZBUF, i, :], adj_hi[:, i, :], start=False, stop=i == NT - 1)
                last.then_inc(node_done, 1)

            def turn_of(b, g, main, side, k=None, last=False):
                for u in range(BODY):
                    if main and not (last and u >= BODY - 2):
                        channel_mix(g, u + 2)
                    side(u)
                    if main:
                        node_mix(b, g, u, first=k == 0 and u == 0)

            def batch(b, main, adjacency, sums, last=False):
                a, r, g = b + 1, b + 2, b * T
                for k in range(2):
                    turn_of(b, g + k * BODY, main, lambda u: adjacency and make(a, u + k * BODY), k)
                if main:
                    with pe.Fori(0, LOOP_TURNS) as turn:
                        turn_of(b, g + turn * BODY + 2 * BODY, main, lambda u: None)
                for k in range(2):
                    turn_of(b, g + (6 + k) * BODY, main, lambda u: sums and project(r, u + k * BODY), last=last and k == 1)

            project_h(0)
            project_wh(0)
            batch(-1, False, True, True)
            channel_mix(0, 0)
            channel_mix(0, 1)
            with pe.Fori(0, B - 2) as b:
                batch(b, True, True, True)
            batch(B - 2, True, True, False)
            batch(B - 1, True, False, False, last=True)

        @block.scalar
        def _(act):
            act.wait_ge(pre, 1)
            nc.scalar.copy(mixT[:, :], ps_adj[:, 0, 0:P]).then_inc(pre_sb, 1)
            act.wait_ge(pre, 2)
            nc.scalar.copy(pT[:, :], ps_adj[:, 1, 0:P]).then_inc(pre_sb, 1)
            act.wait_ge(pre_sb, 2)
            nc.scalar.copy(p_split[:, 0, :], pT[:, :]).then_inc(pre_sb, 1)
            nc.scalar.mul(wb_t[:, :], wb_sb[:, :], float(T))
            act.wait_ge(pre, 3)
            nc.scalar.copy(pb_row[:, :], ps_adj[:, 0, 0:P]).then_inc(pre_sb, 1)
            act.sem_inc(relu_done, RELU0)
            act.wait_ge(pre_sb, 5)

            def take_h(r):
                act.wait_ge(h_ps, r + 1)
                nc.scalar.activation(hT[:, :], ps_adj[:, 0, :], ACT.Identity, bias=wb_t[:, 0:1]).then_inc(h_sb, 1)

            def take_e(r):
                act.wait_ge(wh_ps, r + 1)
                nc.scalar.copy(e_row[:, :], ps_adj[:, 1, :]).then_inc(erow_ready, 1)

            def exps(a, i):
                act.wait_ge(smax_ready, a * NT + (i + 1))
                w = work[:, i, :, :]
                nc.scalar.activation(w.rearrange("p s m -> p (s m)"), ps_adj[:, :, :].rearrange("p s m -> p (s m)"), ACT.Relu, scale=SCALE).then_inc(relu_done, 1)
                act.wait_ge(relu_done, a * NT + (i + 1 + RELU0))
                nc.scalar.activation(w[:, 0, :], w[:, 0, :], ACT.Exp, bias=sneg[:, i, 0:1], accum_out=ssum[:, i, 0:1])
                nc.scalar.activation(w[:, 1, :], w[:, 1, :], ACT.Exp, bias=sneg[:, i, 1:2], accum_out=ssum[:, i, 1:2]).then_inc(exp_done, 1)

            def row_exp(a, i):
                act.wait_ge(lneg_ready, a * NT + (i + 1))
                nc.scalar.activation(prob[:, i, :], prob[:, i, :], ACT.Exp, bias=lneg[:, i:i + 1], accum_out=lsum[:, i:i + 1]).then_inc(lexp_done, 1)

            def normalise(a, i):
                act.wait_ge(lrec_ready, a * NT + (i + 1))
                nc.scalar.mul(prob[:, i, :], prob[:, i, :], lrec[:, i:i + 1]).then_inc(prob_ready, 1)

            def make(a, u):
                for i in at(MAKE_START, u, 1):
                    exps(a, i)
                for i in at(MAKE_START, u, 5):
                    row_exp(a, i)
                for i in at(MAKE_START, u, 6):
                    normalise(a, i)
                if u >= BODY + FIRST:
                    search(a, u - BODY - FIRST, range(HALF))

            def search(a, k, tiles):
                act.wait_ge(cand_ready, a * (SLOTS + 2) + cands(k))
                for i in tiles:
                    last = nc.scalar.activation(sign[:, i, :], prob[:, i, :], ACT.Sign, bias=cand[:, i:i + 1].bitcast(F32), accum_out=count[:, i:i + 1])
                last.then_inc(counted, 1)

            def mask(a, r, u, sums):
                for i in at(MASK_START, u, 1):
                    act.wait_ge(kth_ready, a * NT + (i + 1))
                    nc.scalar.activation(sign[:, i, :], prob[:, i, :], ACT.Sign, bias=kth_neg[:, i:i + 1], accum_out=balance[:, i:i + 1]).then_inc(signed, 1)
                    act.wait_ge(signed, a * NT + (i + 1))
                    nc.scalar.activation(work[:, i, 1, :], sign[:, i, :], ACT.Square, accum_out=unequal[:, i:i + 1]).then_inc(balanced, 1)
                if sums and u == PROJECT_H:
                    take_h(r)
                if sums and u == PROJECT_WH:
                    take_e(r)
                if FIRST <= u < BODY:
                    search(a, BITS + u - FIRST, range(HALF, NT))

            def split_adj(b):
                act.wait_ge(node_done, b * T + NODE0)
                for i in range(NT):
                    act.wait_ge(masked, b * NT + (i + 1))
                    nc.scalar.copy(adj_hi[:, i, :], prob[:, i, :]).then_inc(ahi_ready, 1)

            def split_x(g, u, turns):
                if u % 2 == 0:
                    act.wait_ge(pair_in[u // 2 % PAIRS], (turns + u // BODY) * 16 + 16)
                act.wait_ge(chmix_done, g + (u - 1 + CHMIX0))
                nc.scalar.copy(x_hi[:, u % 2, :], x_in[:, u // 2 % PAIRS, u % 2, :]).then_inc(xh_ready, 1)

            def split_z(g, u):
                act.wait_ge(zsum_ready, g + (u + 1 + ZSUM0))
                act.wait_ge(node_done, g + (u + 1 - ZBUF + NODE0))
                nc.scalar.copy(z_hi[:, u % ZBUF, :, :], zsum[:, :, :]).then_inc(zh_ready, 1)

            def turn_of(b, g, turns, main, side, k=None, last=False):
                for u in range(BODY):
                    if main:
                        if not (last and u >= BODY - 1):
                            split_z(g, u + 1)
                        if k == 0 and u == 0:
                            split_adj(b)
                        if not (last and u >= BODY - 3):
                            split_x(g, u + 3, turns)
                    side(u)

            def batch(b, main, adjacency, sums, last=False):
                a, r, g, n = b + 1, b + 2, b * T, b * TURNS
                for k in range(2):
                    turn_of(b, g + k * BODY, n + k, main, lambda u: adjacency and make(a, u + k * BODY), k)
                with act.Fori(0, LOOP_TURNS) as turn:
                    turn_of(b, g + turn * BODY + 2 * BODY, n + turn + 2, main, lambda u: adjacency and u >= FIRST and search(a, turn * SEARCHES + (SEARCHES + u - FIRST), range(NT)))
                for k in range(2):
                    turn_of(b, g + (6 + k) * BODY, n + 6 + k, main, lambda u: adjacency and mask(a, r, u + k * BODY, sums), last=last and k == 1)

            take_h(0)
            take_e(0)
            batch(-1, False, True, True)
            for u in range(2):
                split_x(0, u, 0)
            split_z(0, 0)
            split_x(0, 2, 0)
            with act.Fori(0, B - 2) as b:
                batch(b, True, True, True)
            batch(B - 2, True, True, False)
            batch(B - 1, True, False, False, last=True)

        @block.gpsimd
        def _(pool):
            pool.sem_inc(row_done, ROW0)
            pool.sem_inc(sums_p, SUMS0)
            for s in range(PAIRS):
                pool.sem_inc(pair_out[s], 16)

            def clear(r):
                if not (isinstance(r, int) and r == 0):
                    pool.wait_ge(h_ps, r)
                    pool.nop(nofuse=True)
                nc.gpsimd.memset(xs_p[:, :], 0.0).then_inc(cleared_p, 1)

            def add(n, slot_half):
                pool.wait_ge(sums_p, n + SUMS0)
                nc.gpsimd.tensor_tensor(xs_p[:, :], xs_p[:, :], stage_p[:, slot_half // 2, slot_half % 2, :], ALU.add).then_inc(sums_p, 1)

            def add_time(r, turn, u):
                if u in POOL_ADDS:
                    j = POOL_ADDS[u]
                    if j == 0:
                        pool.wait_ge(cleared_p, r + 1)
                    if j % 2 == 0:
                        pool.wait_ge(staged_p[j // 2], r * (16 * (LOOP_TURNS + 1)) + turn * 16 + 16)
                    add(r * (T // 2) + turn * (2 * POOL_PAIRS) + j, j)

            def add_last(r, u):
                if u % 2 == 0:
                    fills = LOOP_TURNS + 1 if u // 2 < POOL_PAIRS else 1
                    pool.wait_ge(staged_p[u // 2], r * (16 * fills) + 16 * fills)
                add(r * (T // 2) + (T // 2 - BODY + u), u)

            def make(a, u):
                for i in at(MAKE_START, u, 3):
                    pool.wait_ge(attn_ready, a * NT + (i + 1))
                    w0 = work[:, i, 0, :]
                    nc.gpsimd.tensor_tensor(w0, w0, cwa_sb[:, i, :], ALU.mult).then_inc(weighted, 1)
                    pool.wait_ge(weighted, a * NT + (i + 1))
                    nc.gpsimd.tensor_tensor(prob[:, i, :], prob[:, i, :], w0, ALU.add).then_inc(logit_sum, 1)

            def split_adj(b):
                pool.wait_ge(ahi_ready, b * NT + NT)
                nc.gpsimd.tensor_tensor(adj_lo[:, NT - 1, :], prob[:, NT - 1, :], adj_hi[:, NT - 1, :], ALU.subtract).then_inc(alo_pool, 1)

            def split_x(g, u):
                pool.wait_ge(xh_ready, g + (u + 1))
                nc.gpsimd.tensor_tensor(x_lo[:, u % 2, :], x_in[:, u // 2 % PAIRS, u % 2, :], x_hi[:, u % 2, :], ALU.subtract).then_inc(xl_ready, 1)

            def add_skip(g, u, turns):
                if u % 2 == 0:
                    pool.wait_ge(pair_out[u // 2], turns * 16 + 16)
                pool.wait_ge(scaled_ready, g + (u + 1 + SCALED0))
                nc.gpsimd.tensor_tensor(o_out[:, u // 2, u % 2, :], scaled[:, u % 2, :], x_in[:, u // 2, u % 2, :], ALU.add).then_inc(row_done, 1)

            def turn_of(b, g, turns, main, side, k=None, last=False):
                for u in range(BODY):
                    if main:
                        if k == 0 and u == 0:
                            split_adj(b)
                        if not (last and u >= BODY - 4):
                            split_x(g, u + 4)
                        add_skip(g, u, turns)
                    side(u)

            def batch(b, main, adjacency, sums, last=False):
                a, r, g, n = b + 1, b + 2, b * T, b * TURNS
                if sums:
                    clear(r)
                for k in range(2):
                    turn_of(b, g + k * BODY, n + k, main, lambda u: adjacency and make(a, u + k * BODY), k)
                if main or sums:
                    with pool.Fori(0, LOOP_TURNS) as turn:
                        turn_of(b, g + turn * BODY + 2 * BODY, n + turn + 2, main, lambda u: sums and add_time(r, turn, u))
                for k in range(2):
                    turn_of(b, g + (6 + k) * BODY, n + 6 + k, main, lambda u: sums and k == 0 and add_last(r, u), last=last and k == 1)

            clear(0)
            with pool.Fori(0, LOOP_TURNS) as turn:
                for u in range(BODY):
                    add_time(0, turn, u)
            for u in range(BODY):
                add_last(0, u)
            batch(-1, False, True, True)
            for u in range(4):
                split_x(0, u)
            with pool.Fori(0, B - 2) as b:
                batch(b, True, True, True)
            batch(B - 2, True, True, False)
            batch(B - 1, True, False, False, last=True)

        @block.vector
        def _(dve):
            V = nc.vector
            dve.sem_inc(zsum_ready, ZSUM0)
            dve.sem_inc(zl_ready, ZL0)
            dve.sem_inc(scaled_ready, SCALED0)
            dve.sem_inc(sums_d, SUMS0)

            V.memset(one[:, :], 1.0).then_inc(dve_step, 1)

            steps = [0]

            def step(instruction):
                steps[0] += 1
                instruction.then_inc(dve_step, 1)
                return steps[0]

            def after(a, n):
                dve.wait_ge(dve_step, a * STEPS + (n + 1))

            def clear(r):
                if not (isinstance(r, int) and r == 0):
                    dve.wait_ge(h_ps, r)
                V.memset(xs_d[:, :], 0.0).then_inc(cleared_d, 1)

            def add_time(r, turn, u):
                if u % 2 == 0:
                    dve.wait_ge(staged_d[u // 2], r * (16 * LOOP_TURNS) + turn * 16 + 16)
                if u == 0:
                    dve.wait_ge(cleared_d, r + 1)
                dve.wait_ge(sums_d, r * (T // 2) + turn * BODY + (u + SUMS0))
                V.tensor_tensor(xs_d[:, :], xs_d[:, :], stage_d[:, u // 2, u % 2, :], ALU.add).then_inc(sums_d, 1)

            def take_wh1(r):
                dve.wait_ge(wh_ps, r + 1)
                V.tensor_copy(wh1[:, :], ps_adj[:, 0, 0:NT]).then_inc(wh1_ready, 1)

            def score_max(a, i):
                dve.wait_ge(s_done, a * NT + (i + 1))
                after(a, step(V.tensor_reduce(smax[:, i, :], ps_adj[:, :, :], AX.X, ALU.max)))
                V.tensor_scalar(sneg[:, i, :], smax[:, i, :], 0.0, -SCALE, ALU.max, ALU.mult).then_inc(smax_ready, 1)

            def attention(a, i, main):
                dve.wait_ge(exp_done, a * NT + (i + 1))
                if i == 0:
                    if main:
                        dve.wait_ge(alo_dve, a * (NT - 1))
                        dve.wait_ge(alo_pool, a)
                    dve.wait_ge(erow_ready, a + 1)
                    dve.wait_ge(wh1_ready, a + 1)
                w0, w1 = work[:, i, 0, :], work[:, i, 1, :]
                n = step(V.reciprocal(coef[:, i, :], ssum[:, i, :]))
                step(V.scalar_tensor_tensor(prob[:, i, :], e_row[:, :], wh1[:, i:i + 1], cw_sb[:, i, :], ALU.add, ALU.mult))
                after(a, n)
                after(a, step(V.tensor_tensor(coef[:, i, :], coef[:, i, :], fc_sb[:, 0:2], ALU.mult)))
                after(a, step(V.tensor_scalar(w1, w1, coef[:, i, 1:2], fc_sb[:, 2:3], ALU.mult, ALU.add)))
                V.scalar_tensor_tensor(w0, w0, coef[:, i, 0:1], w1, ALU.mult, ALU.add).then_inc(attn_ready, 1)

            def row_max(a, i):
                dve.wait_ge(logit_sum, a * NT + (i + 1))
                after(a, step(V.tensor_reduce(lmax[:, i:i + 1], prob[:, i, :], AX.X, ALU.max)))
                V.tensor_scalar(lneg[:, i:i + 1], lmax[:, i:i + 1], -1.0, None, ALU.mult).then_inc(lneg_ready, 1)

            def make(a, u, main):
                for i in at(MAKE_START, u, 0):
                    score_max(a, i)
                for i in at(MAKE_START, u, 2):
                    attention(a, i, main)
                for i in at(MAKE_START, u, 4):
                    row_max(a, i)
                for i in at(MAKE_START, u, 5):
                    dve.wait_ge(lexp_done, a * NT + (i + 1))
                    V.reciprocal(lrec[:, i:i + 1], lsum[:, i:i + 1]).then_inc(lrec_ready, 1)
                if u == BODY + 1:
                    start_search(a, 0)
                if u >= BODY + FIRST:
                    search(a, u - BODY - FIRST, [(0, u - BODY - FIRST)])
                if u == 2 * BODY - 1:
                    start_search(a, 1)

            def start_search(a, half):
                c = slice(half * HALF, half * HALF + HALF)
                dve.wait_ge(prob_ready, a * NT + half * HALF + HALF)
                V.tensor_copy(cand[:, c], cand0_sb[:, c]).then_inc(cand_ready, 1)

            def search(a, k, halves):
                dve.wait_ge(counted, a * SLOTS + k + 1)
                for half, bit in halves:
                    c = slice(half * HALF, half * HALF + HALF)
                    last = V.tensor_scalar(miss[:, c], count[:, c], float(ENOUGH), bitf_sb[:, bass.ds(bit, 1)], ALU.is_lt, ALU.mult)
                last.then_inc(missed, 1)
                dve.wait_ge(missed, a * SLOTS + k + 1)
                for half, bit in halves:
                    c = slice(half * HALF, half * HALF + HALF)
                    last = V.scalar_tensor_tensor(cand[:, c], miss[:, c], biti_sb[:, bass.ds(bit + 1, 1)], cand[:, c], ALU.bitwise_xor, ALU.bitwise_xor)
                last.then_inc(cand_ready, 1)

            def mask(a, r, u, sums):
                for half in range(2):
                    if u == MASK_START[half * HALF]:
                        c = slice(half * HALF, half * HALF + HALF)
                        dve.wait_ge(cand_ready, a * (SLOTS + 2) + cands(BITS + half * SEARCHES))
                        after(a, step(V.tensor_scalar(thr[:, c], cand[:, c].bitcast(F32), -1.0, None, ALU.mult)))
                for i in at(MASK_START, u, 0):
                    p, w = prob[:, i, :], work[:, i, 0, :]
                    after(a, step(V.scalar_tensor_tensor(w, p, thr[:, i:i + 1], p, ALU.is_lt, ALU.add)))
                    after(a, step(V.tensor_reduce(kth[:, i:i + 1], w, AX.X, ALU.min)))
                    V.tensor_scalar(kth_neg[:, i:i + 1], kth[:, i:i + 1], -1.0, None, ALU.mult).then_inc(kth_ready, 1)
                for i in at(MASK_START, u, 2):
                    w, squares = work[:, i, 0, :], work[:, i, 1, :]
                    dve.wait_ge(balanced, a * NT + (i + 1))
                    step(V.tensor_tensor_scan(w, squares, one[:, 0:1].to_broadcast([P, N]), 0.0, ALU.add, ALU.subtract))
                    after(a, step(V.tensor_tensor(ties_neg[:, i:i + 1], balance[:, i:i + 1], unequal[:, i:i + 1], ALU.add)))
                    step(V.tensor_scalar(ties_neg[:, i:i + 1], ties_neg[:, i:i + 1], 0.5, -float(KEEP), ALU.mult, ALU.add))
                for i in at(MASK_START, u, 3):
                    p, w = prob[:, i, :], work[:, i, 0, :]
                    after(a, steps[0])
                    after(a, step(V.scalar_tensor_tensor(w, sign[:, i, :], BIG, w, ALU.mult, ALU.add)))
                    V.scalar_tensor_tensor(p, w, ties_neg[:, i:i + 1], p, ALU.is_ge, ALU.mult).then_inc(masked, 1)
                if FIRST <= u < BODY:
                    search(a, BITS + u - FIRST, [(1, BITS - SEARCHES + u - FIRST)])
                if sums and u == PROJECT_WH:
                    take_wh1(r)

            def split_adj(b):
                for i in range(NT - 1):
                    dve.wait_ge(ahi_ready, b * NT + (i + 1))
                    V.tensor_tensor(adj_lo[:, i, :], prob[:, i, :], adj_hi[:, i, :], ALU.subtract).then_inc(alo_dve, 1)

            def sum_z(g, u):
                v = ps_mix[u % 2][:, :].rearrange("p (i s d) -> p i s d", i=NT, s=2)
                dve.wait_ge(chmix_done, g + (u + 1 + CHMIX0))
                dve.wait_ge(zl_ready, g + (u + ZL0))
                V.tensor_tensor(zsum[:, :, :], v[:, :, 1, :], pb_row[:, :].rearrange("p (o d) -> p o d", o=1).to_broadcast([P, NT, P]), ALU.add).then_inc(zpart, 1)
                dve.wait_ge(zpart, g + (u + 1))
                V.tensor_tensor(zsum[:, :, :], v[:, :, 0, :], zsum[:, :, :], ALU.add).then_inc(zsum_ready, 1)

            def split_z(g, u):
                dve.wait_ge(zh_ready, g + (u + 1))
                V.tensor_tensor(z_lo[:, u % ZBUF, :, :], zsum[:, :, :], z_hi[:, u % ZBUF, :, :], ALU.subtract).then_inc(zl_ready, 1)

            def scale_out(g, u):
                dve.wait_ge(node_done, g + (u + 1 + NODE0))
                dve.wait_ge(row_done, g + (u - 1 + ROW0))
                V.scalar_tensor_tensor(scaled[:, u % 2, :], ps_out[u % 2][:, :], cb_sb[:, 0:1], emb_sb[:, :], ALU.add, ALU.mult).then_inc(scaled_ready, 1)

            def turn_of(b, g, main, side, k=None, last=False):
                for u in range(BODY):
                    z = main and not (last and u >= BODY - 2)
                    if main and k == 0 and u == 0:
                        split_adj(b)
                    if z:
                        sum_z(g, u + 2)
                    side(u)
                    if z:
                        split_z(g, u + 2)
                    if main:
                        scale_out(g, u)

            def batch(b, main, adjacency, sums, last=False):
                a, r, g = b + 1, b + 2, b * T
                steps[0] = 0
                if sums:
                    clear(r)
                for k in range(2):
                    turn_of(b, g + k * BODY, main, lambda u: adjacency and make(a, u + k * BODY, main), k)
                with dve.Fori(0, LOOP_TURNS) as turn:
                    def side(u):
                        if sums:
                            add_time(r, turn, u)
                        if adjacency and u >= FIRST:
                            first, second = turn * SEARCHES + (SEARCHES + u - FIRST), turn * SEARCHES + (u - FIRST)
                            search(a, first, [(0, first), (1, second)])
                    turn_of(b, g + turn * BODY + 2 * BODY, main, side)
                for k in range(2):
                    turn_of(b, g + (6 + k) * BODY, main, lambda u: adjacency and mask(a, r, u + k * BODY, sums), last=last and k == 1)
                assert steps[0] == (STEPS if adjacency else 0), steps

            clear(0)
            with dve.Fori(0, LOOP_TURNS) as turn:
                for u in range(BODY):
                    add_time(0, turn, u)
            dve.wait_ge(pre_sb, 4)
            V.tensor_tensor(p_split[:, 1, :], pT[:, :], p_split[:, 0, :], ALU.subtract).then_inc(pre_sb, 1)
            take_wh1(0)
            batch(-1, False, True, True)
            for u in range(2):
                sum_z(0, u)
                split_z(0, u)
            with dve.Fori(0, B - 2) as b:
                batch(b, True, True, True)
            batch(B - 2, True, True, False)
            batch(B - 1, True, False, False, last=True)


def kernel(**inputs):
    from concourse import bacc
    from concourse.bass_utils import run_bass_kernel_spmd

    v = {k: np.asarray(w) for k, w in inputs.items()}
    t = lambda m: np.ascontiguousarray(m.T)
    pow2 = np.append(2.0 ** np.arange(BITS - 1, -1, -1), 0.0)
    data = [
        ("x", v["x"].transpose(0, 3, 1, 2).reshape(B, T // 2, 2, C, N).transpose(0, 1, 3, 2, 4)),
        ("w_nat", v["L0_conv_W_w"]),
        ("w_t", t(v["L0_conv_W_w"])),
        ("w_b", v["L0_conv_W_b"].reshape(C, 1)),
        ("theta_t", t(v["L0_conv_theta"])),
        ("conv_t", t(v["L0_conv_conv_w"])),
        ("conv_b", v["L0_conv_conv_b"].reshape(C, 1)),
        ("mem_t", t(v["L0_conv_memory"])),
        ("a_vec", t(v["L0_conv_a_vec"].reshape(2, C))),
        ("cw", v["L0_conv_cw"]),
        ("cwa", v["L0_conv_cwa"]),
        ("fc", np.concatenate([v["L0_conv_fc_w"].reshape(1, 2), v["L0_conv_fc_b"].reshape(1, 1)], axis=1)),
        ("emb", v["L0_conv_emb"].reshape(C, N)),
        ("bits_f", np.tile(pow2.astype(np.float32), (P, 1))),
        ("bits_i", np.tile(pow2.astype(np.int32), (P, 1))),
        ("cand0", np.full((P, NT), -2 ** 31 + 2 ** (BITS - 1), np.int32)),
    ]
    nc = bacc.Bacc("TRN2", target_bir_lowering=False, num_devices=1)
    arrays, args = {}, []
    for name, w in data:
        w = np.ascontiguousarray(w)
        arrays[name + "_dram"] = w
        args.append(nc.dram_tensor(name + "_dram", w.shape, mybir.dt.from_np(w.dtype), kind="ExternalInput").ap())
    out = nc.dram_tensor("out_dram", (B, T // 2, C, 2, N), F32, kind="ExternalOutput").ap()
    build(nc, *args, out)
    r = run_bass_kernel_spmd(nc, [arrays], core_ids=[0])
    o = r.results[0]["out_dram"]
    return np.ascontiguousarray(o.transpose(0, 2, 4, 1, 3).reshape(B, C, N, T))
```

```python
from contextlib import ExitStack

import numpy as np
import concourse.bass as bass
from concourse import mybir

F32 = mybir.dt.float32
F32R = mybir.dt.float32r
I32 = mybir.dt.int32
ALU = mybir.AluOpType
ACT = mybir.ActivationFunctionType
AX = mybir.AxisListType

B, C, N, T = 8, 128, 512, 64
P = 128
NT = N // P
KEEP = int(N * 0.8)
SCALE = float(np.float32(1.0) / np.sqrt(np.float32(C)))

BODY = 8
TURNS = T // BODY
LOOP_TURNS = 4
HALF = NT // 2
PAIRS = BODY // 2
POOL_PAIRS = 3
SPAN = PAIRS + POOL_PAIRS
POOL_ADDS = {0: 0, 1: 1, 2: 2, 4: 3, 5: 4, 6: 5}
SEARCHES = 6
BITS = (LOOP_TURNS + 1) * SEARCHES
FIRST = BODY - SEARCHES
COUNTS = [[(0, 0, 0), (0, 1, 0), (1, 0, 0)], [(1, 1, 0), (0, 0, 1), (0, 1, 1)],
          [(1, 0, 1), (1, 1, 1), (0, 0, 2)], [(0, 1, 2), (1, 0, 2), (1, 1, 2)]]
ENOUGH = 2 * KEEP - 1 - N

XBUF = ZBUF = 4
BIG = 2.0 * N
Q = 32

CHMIX0, ZSUM0, ZL0, NODE0, SCALED0, ROW0, RELU0, SUMS0 = 4, 2, 1, 4, 2, 2, 1, 1

STEPS = 58


def build(nc, x, w_nat, w_t, w_b, theta_t, conv_t, conv_b, mem_t, a_vec, cw, cwa, fc, emb, bits_f, bits_i, cand0, out):
    with ExitStack() as ctx:
        def sb(name, shape, dt=F32):
            return ctx.enter_context(nc.sbuf_tensor(name, shape, dt))

        def ps(name, shape):
            return ctx.enter_context(nc.psum_tensor(name, shape, F32))

        def sem(name):
            return ctx.enter_context(nc.semaphore(name))

        x_in = sb("x_in", [P, PAIRS, 2, N])
        o_out = sb("o_out", [P, PAIRS, 2, N])
        stage_d = sb("stage_d", [P, PAIRS, 2, N])
        stage_p = sb("stage_p", [P, PAIRS, 2, N])
        xs_d = sb("xs_d", [P, N])
        xs_p = sb("xs_p", [P, N])
        adj_hi = sb("adj_hi", [P, NT, N], F32R)
        adj_lo = sb("adj_lo", [P, NT, N], F32R)
        prob = sb("prob", [P, NT, N])
        work = sb("work", [P, NT, 2, N])
        cw_sb = sb("cw_sb", [P, NT, N])
        cwa_sb = sb("cwa_sb", [P, NT, N])
        x_hi = sb("x_hi", [P, XBUF, N], F32R)
        x_lo = sb("x_lo", [P, XBUF, N], F32R)
        zpart = sb("zpart", [P, NT, P])
        zsum = sb("zsum", [P, NT, P])
        z_hi = sb("z_hi", [P, ZBUF, NT, P], F32R)
        z_lo = sb("z_lo", [P, ZBUF, NT, P], F32R)
        scaled = sb("scaled", [P, 2, N])
        hT = sb("hT", [P, N])
        e_row = sb("e_row", [P, N])
        emb_sb = sb("emb_sb", [P, N])
        memT_sb = sb("memT_sb", [P, N])
        wT_sb = sb("wT_sb", [P, P])
        w_sb = sb("w_sb", [P, P])
        thT_sb = sb("thT_sb", [P, P])
        cvT_sb = sb("cvT_sb", [P, P])
        mixT = sb("mixT", [P, P])
        pT = sb("pT", [P, P])
        p_split = sb("p_split", [P, 2, P], F32R)
        chosen = sb("chosen", [P, 3 * Q])
        chosen_r = sb("chosen_r", [P, 3 * Q], F32R)
        pb_parts = sb("pb_parts", [3 * Q, P], F32R)
        colsum = sb("colsum", [3 * Q, N], F32R)
        pb_row = sb("pb_row", [P, P])
        wb_sb = sb("wb_sb", [P, 1])
        wb_t = sb("wb_t", [P, 1])
        cb_sb = sb("cb_sb", [P, 1])
        a_sb = sb("a_sb", [P, 2])
        fc_sb = sb("fc_sb", [P, 3])
        bitf_sb = sb("bitf_sb", [P, BITS + 1])
        biti_sb = sb("biti_sb", [P, BITS + 1], I32)
        cand0_sb = sb("cand0_sb", [P, NT], I32)
        cand = sb("cand", [P, NT], I32)
        miss = sb("miss", [P, NT], I32)
        count = sb("count", [P, NT])
        thr = sb("thr", [P, NT])
        kth = sb("kth", [P, NT])
        kth_neg = sb("kth_neg", [P, NT])
        balance = sb("balance", [P, NT])
        unequal = sb("unequal", [P, NT])
        ties_neg = sb("ties_neg", [P, NT])
        smax = sb("smax", [P, NT, 2])
        sneg = sb("sneg", [P, NT, 2])
        ssum = sb("ssum", [P, NT, 2])
        coef = sb("coef", [P, NT, 2])
        lmax = sb("lmax", [P, NT])
        lneg = sb("lneg", [P, NT])
        lsum = sb("lsum", [P, NT])
        lrec = sb("lrec", [P, NT])
        wh1 = sb("wh1", [P, NT])
        one = sb("one", [P, 1])
        sign = sb("sign", [P, NT, N])

        ps_mix = [ps(f"ps_mix{i}", [P, 2 * N]) for i in range(2)]
        ps_out = [ps(f"ps_out{i}", [P, N]) for i in range(2)]
        ps_adj = ps("ps_adj", [P, 2, N])

        consts_in = sem("consts_in")
        pair_in = [sem(f"pair_in{i}") for i in range(PAIRS)]
        pair_out = [sem(f"pair_out{i}") for i in range(PAIRS)]
        staged_d = [sem(f"staged_d{i}") for i in range(PAIRS)]
        staged_p = [sem(f"staged_p{i}") for i in range(PAIRS)]
        chosen_set = sem("chosen_set")
        pre = sem("pre")
        pre_sb = sem("pre_sb")
        xh_ready = sem("xh_ready")
        xl_ready = sem("xl_ready")
        chmix_done = sem("chmix_done")
        part_ready = sem("part_ready")
        colsum_done = sem("colsum_done")
        colsum_hi = sem("colsum_hi")
        colsum_split = sem("colsum_split")
        zsum_ready = sem("zsum_ready")
        zh_ready = sem("zh_ready")
        zl_ready = sem("zl_ready")
        node_done = sem("node_done")
        scaled_ready = sem("scaled_ready")
        row_done = sem("row_done")
        cleared_d = sem("cleared_d")
        cleared_p = sem("cleared_p")
        sums_d = sem("sums_d")
        sums_p = sem("sums_p")
        h_ps = sem("h_ps")
        h_sb = sem("h_sb")
        wh_ps = sem("wh_ps")
        erow_ready = sem("erow_ready")
        wh1_ready = sem("wh1_ready")
        s_done = sem("s_done")
        smax_ready = sem("smax_ready")
        relu_done = sem("relu_done")
        exp_done = sem("exp_done")
        attn_ready = sem("attn_ready")
        logit_sum = sem("logit_sum")
        lneg_ready = sem("lneg_ready")
        lexp_done = sem("lexp_done")
        prob_ready = sem("prob_ready")
        counted = [sem(f"counted{i}") for i in range(2)]
        missed = [sem(f"missed{i}") for i in range(2)]
        cand_ready = [sem(f"cand_ready{i}") for i in range(2)]
        kth_ready = sem("kth_ready")
        signed = sem("signed")
        balanced = sem("balanced")
        masked = sem("masked")
        adj_used = sem("adj_used")
        ahi_ready = sem("ahi_ready")
        alo_ready = sem("alo_ready")
        dve_step = sem("dve_step")

        N_CONST = 16 * 15
        MAKE_START = [0, 2, 5, 8]
        MASK_START = [0, 3, BODY, BODY + 3]
        PROJECT_H, PROJECT_WH = BODY + 2, BODY + 4

        def at(start, u, offset):
            return [i for i in range(NT) if start[i] + offset == u]

        block = ctx.enter_context(nc.Block())

        @block.sync
        def _(sp):
            def load_x(g_pair, s):
                sp.dma_start(x_in[:, s, :, :], x_flat[g_pair]).then_inc(pair_in[s], 16)

            x_flat = x.rearrange("b q c k n -> (b q) c k n")
            o_flat = out.rearrange("b q c k n -> (b q) c k n")

            def stream_d(r, turn, s):
                sp.dma_start(stage_d[:, s, :, :], x[r, turn * SPAN + s]).then_inc(staged_d[s], 16)

            def stream_p(r, turn, s):
                sp.dma_start(stage_p[:, s, :, :], x[r, turn * SPAN + (PAIRS + s)]).then_inc(staged_p[s], 16)

            def stream_last(r, s):
                sp.dma_start(stage_p[:, s, :, :], x[r, LOOP_TURNS * SPAN + s]).then_inc(staged_p[s], 16)

            def summed(r, turn, s):
                sp.wait_ge(sums_d, r * (T // 2) + turn * BODY + (2 * s + 2 + SUMS0))
                sp.nop(nofuse=True)
                if s < POOL_PAIRS:
                    sp.wait_ge(sums_p, r * (T // 2) + turn * (2 * POOL_PAIRS) + (2 * s + 2 + SUMS0))
                sp.nop(nofuse=True)

            def next_stream(r, turn, s):
                summed(r, turn, s)
                stream_d(r, turn + 1, s)
                if s < POOL_PAIRS:
                    stream_p(r, turn + 1, s)

            def last_stream(r, s):
                if s < POOL_PAIRS:
                    summed(r, LOOP_TURNS - 1, s)
                stream_last(r, s)

            for s in range(PAIRS):
                stream_d(0, 0, s)
                if s < POOL_PAIRS:
                    stream_p(0, 0, s)
            for dst, src in ((w_sb, w_nat), (wT_sb, w_t), (thT_sb, theta_t), (cvT_sb, conv_t), (memT_sb, mem_t),
                             (emb_sb, emb), (wb_sb, w_b), (cb_sb, conv_b), (a_sb, a_vec), (bitf_sb, bits_f),
                             (biti_sb, bits_i), (cand0_sb, cand0)):
                sp.dma_start(dst[:, :], src).then_inc(consts_in, 16)
            sp.dma_start(fc_sb[:, :], fc.to_broadcast([P, 3])).then_inc(consts_in, 16)
            with sp.Fori(0, LOOP_TURNS - 1) as turn:
                for s in range(PAIRS):
                    next_stream(0, turn, s)
            for s in range(PAIRS):
                last_stream(0, s)
            for dst, src in ((cw_sb, cw), (cwa_sb, cwa)):
                sp.dma_start(dst[:, :, :], src.rearrange("(i p) m -> p i m", p=P)).then_inc(consts_in, 16)
            for s in range(PAIRS):
                load_x(s, s)

            def move(g_pair, s, last=False):
                sp.wait_ge(row_done, g_pair * 2 + (2 * s + 2 + ROW0))
                sp.dma_start(o_flat[g_pair + s], o_out[:, s, :, :]).then_inc(pair_out[s], 16)
                if not last:
                    load_x(g_pair + (PAIRS + s), s)

            def batch(b, main, sums, last=False):
                g_pair = b * (T // 2)
                r = b + 2
                if sums:
                    sp.wait_ge(sums_d, r * (T // 2) + SUMS0)
                    sp.nop(nofuse=True)
                    sp.wait_ge(sums_p, r * (T // 2) + SUMS0)
                    sp.nop(nofuse=True)
                    for s in range(PAIRS):
                        stream_d(r, 0, s)
                        if s < POOL_PAIRS:
                            stream_p(r, 0, s)
                if main:
                    for k in range(2):
                        for s in range(PAIRS):
                            move(g_pair + k * PAIRS, s)
                if sums or main:
                    with sp.Fori(0, LOOP_TURNS - 1) as turn:
                        for s in range(PAIRS):
                            if main:
                                move(g_pair + turn * PAIRS + 2 * PAIRS, s)
                            if sums:
                                next_stream(r, turn, s)
                for k in (5, 6, 7):
                    for s in range(PAIRS):
                        if main:
                            move(g_pair + k * PAIRS, s, last and k == 7)
                        if sums and k == 5:
                            last_stream(r, s)

            batch(-1, False, True)
            with sp.Fori(0, B - 2) as b:
                batch(b, True, True)
            batch(B - 2, True, False)
            batch(B - 1, True, False, last=True)
            for s in range(PAIRS):
                sp.wait_ge(pair_out[s], 16 * (B * TURNS + 1))

        @block.tensor
        def _(pe):
            pe.sem_inc(chmix_done, CHMIX0)
            pe.sem_inc(node_done, NODE0)
            pe.sem_inc(adj_used, NT)
            pe.wait_ge(consts_in, N_CONST)
            nc.tensor.matmul(ps_adj[:, 0, 0:P], thT_sb[:, :], cvT_sb[:, :], start=True, stop=True).then_inc(pre, 1)
            pe.wait_ge(pre_sb, 1)
            nc.tensor.matmul(ps_adj[:, 1, 0:P], w_sb[:, :], mixT[:, :], start=True, stop=True).then_inc(pre, 1)
            pe.wait_ge(pre_sb, 2)
            nc.tensor.matmul(ps_adj[:, 0, 0:P], wb_sb[:, 0:1].to_broadcast([P, P]), mixT[:, :], start=True, stop=True).then_inc(pre, 1)
            pe.wait_ge(pre_sb, 7)
            pe.wait_ge(chosen_set, 3)

            def project_h(r):
                pe.wait_ge(sums_d, r * (T // 2) + (T // 2 + SUMS0))
                pe.wait_ge(sums_p, r * (T // 2) + (T // 2 + SUMS0))
                pe.wait_ge(relu_done, r * NT + RELU0)
                nc.tensor.matmul(ps_adj[:, 0, :], wT_sb[:, :], xs_d[:, :], start=True, stop=False)
                nc.tensor.matmul(ps_adj[:, 0, :], wT_sb[:, :], xs_p[:, :], start=False, stop=True).then_inc(h_ps, 1)

            def project_wh(r):
                pe.wait_ge(h_sb, r + 1)
                nc.tensor.matmul(ps_adj[:, 1, :], a_sb[:, 1:2].to_broadcast([P, P]), hT[:, :], start=True, stop=True)
                for i in range(NT):
                    last = nc.tensor.matmul(ps_adj[:, 0, i:i + 1], hT[:, i * P:(i + 1) * P], a_sb[:, 0:1], start=True, stop=True)
                last.then_inc(wh_ps, 1)

            def scores(a, i, main):
                if i == 0:
                    if main:
                        pe.wait_ge(colsum_split, a)
                    pe.wait_ge(erow_ready, a + 1)
                    pe.wait_ge(wh1_ready, a + 1)
                else:
                    pe.wait_ge(relu_done, a * NT + i + RELU0)
                h_i = hT[:, i * P:(i + 1) * P]
                nc.tensor.matmul(ps_adj[:, 0, :], h_i, memT_sb[:, :], start=True, stop=True)
                nc.tensor.matmul(ps_adj[:, 1, :], h_i, hT[:, :], start=True, stop=True).then_inc(s_done, 1)

            def make(a, u, main):
                for i in at(MAKE_START, u, 0):
                    scores(a, i, main)

            def project(r, u):
                if u == PROJECT_H:
                    project_h(r)
                if u == PROJECT_WH:
                    project_wh(r)

            def channel_mix(g, u):
                pe.wait_ge(xl_ready, g + (u + 1))
                pe.wait_ge(zsum_ready, g + (u - 1 + ZSUM0))
                o = ps_mix[u % 2]
                for i in range(NT):
                    c = i * 2 * P
                    nc.tensor.matmul(o[:, c:c + 2 * P], x_hi[:, u % XBUF, i * P:(i + 1) * P], p_split[:, :, :].rearrange("p s d -> p (s d)"), start=True, stop=False)
                    last = nc.tensor.matmul(o[:, c:c + P], x_lo[:, u % XBUF, i * P:(i + 1) * P], p_split[:, 0, :], start=False, stop=True)
                last.then_inc(chmix_done, 1)

            def node_mix(b, g, u, first=False, final=False, adjacency=False):
                pe.wait_ge(zl_ready, g + (u + 1 + ZL0))
                pe.wait_ge(scaled_ready, g + (u - 1 + SCALED0))
                o = ps_out[u % 2][:, :]
                sums = ps_adj[0:3 * Q, 1, :]
                if first and adjacency:
                    pe.wait_ge(erow_ready, b + 2)
                elif first:
                    pe.wait_ge(relu_done, B * NT + RELU0)
                for i in range(NT):
                    if first:
                        pe.wait_ge(alo_ready, b * NT + (i + 1))
                        nc.tensor.matmul(sums, chosen_r[:, :], adj_hi[:, i, :], start=i == 0, stop=False)
                        last = nc.tensor.matmul(sums, chosen_r[:, :], adj_lo[:, i, :], start=False, stop=i == NT - 1)
                        if i == NT - 1:
                            last.then_inc(colsum_done, 1)
                    nc.tensor.matmul(o, z_hi[:, u % ZBUF, i, :], adj_hi[:, i, :], start=i == 0, stop=False)
                    nc.tensor.matmul(o, z_hi[:, u % ZBUF, i, :], adj_lo[:, i, :], start=False, stop=False)
                    last = nc.tensor.matmul(o, z_lo[:, u % ZBUF, i, :], adj_hi[:, i, :], start=False, stop=False)
                    if final:
                        last.then_inc(adj_used, 1)

            def add_bias(b, u, first):
                if first:
                    pe.wait_ge(colsum_split, b + 1)
                nc.tensor.matmul(ps_out[u % 2][:, :], pb_parts[:, :], colsum[:, :], start=False, stop=True).then_inc(node_done, 1)

            def turn_of(b, g, main, side, k=None, last=False, adjacency=False):
                for u in range(BODY):
                    first = k == 0 and u == 0
                    if main and first:
                        node_mix(b, g, u, first=True, adjacency=adjacency)
                    if main and not (last and u >= BODY - 2):
                        channel_mix(g, u + 2)
                    side(u)
                    if main and not first:
                        node_mix(b, g, u, final=k == 7 and u == BODY - 1)
                    if main:
                        add_bias(b, u, first)

            def batch(b, main, adjacency, sums, last=False):
                a, r, g = b + 1, b + 2, b * T
                for k in range(2):
                    turn_of(b, g + k * BODY, main, lambda u: adjacency and make(a, u + k * BODY, main), k, adjacency=adjacency)
                if main:
                    with pe.Fori(0, LOOP_TURNS) as turn:
                        turn_of(b, g + turn * BODY + 2 * BODY, main, lambda u: None)
                for k in range(2):
                    turn_of(b, g + (6 + k) * BODY, main, lambda u: sums and project(r, u + k * BODY), 6 + k, last=last and k == 1)

            project_h(0)
            project_wh(0)
            batch(-1, False, True, True)
            channel_mix(0, 0)
            channel_mix(0, 1)
            with pe.Fori(0, B - 2) as b:
                batch(b, True, True, True)
            batch(B - 2, True, True, False)
            batch(B - 1, True, False, False, last=True)

        @block.scalar
        def _(act):
            act.wait_ge(pre, 1)
            nc.scalar.copy(mixT[:, :], ps_adj[:, 0, 0:P]).then_inc(pre_sb, 1)
            act.wait_ge(pre, 2)
            nc.scalar.copy(pT[:, :], ps_adj[:, 1, 0:P]).then_inc(pre_sb, 1)
            act.wait_ge(pre_sb, 2)
            nc.scalar.copy(p_split[:, 0, :], pT[:, :]).then_inc(pre_sb, 1)
            nc.scalar.mul(wb_t[:, :], wb_sb[:, :], float(T))
            act.wait_ge(pre, 3)
            nc.scalar.copy(pb_row[:, :], ps_adj[:, 0, 0:P]).then_inc(pre_sb, 1)
            act.wait_ge(pre_sb, 4)
            nc.scalar.copy(pb_parts[:, :], pb_row[0:3 * Q, :]).then_inc(pre_sb, 1)
            act.sem_inc(relu_done, RELU0)
            act.wait_ge(pre_sb, 7)

            def take_h(r):
                act.wait_ge(h_ps, r + 1)
                nc.scalar.activation(hT[:, :], ps_adj[:, 0, :], ACT.Identity, bias=wb_t[:, 0:1]).then_inc(h_sb, 1)

            def take_e(r):
                act.wait_ge(wh_ps, r + 1)
                nc.scalar.copy(e_row[:, :], ps_adj[:, 1, :]).then_inc(erow_ready, 1)

            def relu(a, i):
                act.wait_ge(s_done, a * NT + (i + 1))
                nc.scalar.activation(work[:, i, :, :].rearrange("p s m -> p (s m)"), ps_adj[:, :, :].rearrange("p s m -> p (s m)"), ACT.Relu, scale=SCALE).then_inc(relu_done, 1)

            def exps(a, i):
                act.wait_ge(smax_ready, a * NT + (i + 1))
                w = work[:, i, :, :]
                nc.scalar.activation(w[:, 0, :], w[:, 0, :], ACT.Exp, bias=sneg[:, i, 0:1], accum_out=ssum[:, i, 0:1])
                nc.scalar.activation(w[:, 1, :], w[:, 1, :], ACT.Exp, bias=sneg[:, i, 1:2], accum_out=ssum[:, i, 1:2]).then_inc(exp_done, 1)

            def row_exp(a, i):
                act.wait_ge(lneg_ready, a * NT + (i + 1))
                nc.scalar.activation(prob[:, i, :], prob[:, i, :], ACT.Exp, bias=lneg[:, i:i + 1], accum_out=lsum[:, i:i + 1]).then_inc(lexp_done, 1)

            def make(a, u):
                for i in at(MAKE_START, u, 1):
                    relu(a, i)
                for i in at(MAKE_START, u, 2):
                    exps(a, i)
                for i in at(MAKE_START, u, 6):
                    row_exp(a, i)
                if u >= BODY + FIRST:
                    search(a, 0, u - BODY - FIRST)

            def count_tile(a, half, tile, bit):
                i = half * HALF + tile
                if tile == 0:
                    act.wait_ge(cand_ready[half], a * (BITS + 1) + bit + 1)
                last = nc.scalar.activation(sign[:, i, :], prob[:, i, :], ACT.Sign, bias=cand[:, i:i + 1].bitcast(F32), accum_out=count[:, i:i + 1])
                if tile == HALF - 1:
                    last.then_inc(counted[half], 1)

            def search(a, half, bit):
                for tile in range(HALF):
                    count_tile(a, half, tile, bit)

            def search_both(a, turn, u):
                for half, tile, n in COUNTS[u % 4]:
                    count_tile(a, half, tile, turn * SEARCHES + (u // 4 * 3 + n + (SEARCHES if half == 0 else 0)))

            def mask(a, r, u, sums):
                for i in at(MASK_START, u, 1):
                    act.wait_ge(kth_ready, a * NT + (i + 1))
                    nc.scalar.activation(sign[:, i, :], prob[:, i, :], ACT.Sign, bias=kth_neg[:, i:i + 1], accum_out=balance[:, i:i + 1]).then_inc(signed, 1)
                    act.wait_ge(signed, a * NT + (i + 1))
                    nc.scalar.activation(work[:, i, 1, :], sign[:, i, :], ACT.Square, accum_out=unequal[:, i:i + 1]).then_inc(balanced, 1)
                if sums and u == PROJECT_H + 1:
                    take_h(r)
                if sums and u == PROJECT_WH + 1:
                    take_e(r)
                if FIRST <= u < BODY:
                    search(a, 1, BITS - SEARCHES + u - FIRST)

            def split_adj(b):
                for i in range(NT):
                    act.wait_ge(adj_used, b * NT + (i + 1))
                    act.wait_ge(masked, b * NT + (i + 1))
                    nc.scalar.copy(adj_hi[:, i, :], prob[:, i, :]).then_inc(ahi_ready, 1)

            def take_colsum(b):
                act.wait_ge(colsum_done, b + 1)
                act.wait_ge(node_done, b * T + NODE0)
                nc.scalar.copy(colsum[:, :], ps_adj[0:3 * Q, 1, :]).then_inc(colsum_hi, 1)

            def split_x(g, u, turns):
                if u % 2 == 0:
                    act.wait_ge(pair_in[u // 2 % PAIRS], (turns + u // BODY) * 16 + 16)
                act.wait_ge(chmix_done, g + (u + 1 - XBUF + CHMIX0))
                nc.scalar.copy(x_hi[:, u % XBUF, :], x_in[:, u // 2 % PAIRS, u % 2, :]).then_inc(xh_ready, 1)

            def take_part(g, u):
                v = ps_mix[u % 2][:, :].rearrange("p (i s d) -> p i s d", i=NT, s=2)
                act.wait_ge(chmix_done, g + (u + 1 + CHMIX0))
                act.wait_ge(zsum_ready, g + (u + ZSUM0))
                nc.scalar.copy(zpart[:, :, :], v[:, :, 1, :]).then_inc(part_ready, 1)

            def split_z(g, u):
                act.wait_ge(zsum_ready, g + (u + 1 + ZSUM0))
                act.wait_ge(node_done, g + (u + 1 - ZBUF + NODE0))
                nc.scalar.copy(z_hi[:, u % ZBUF, :, :], zsum[:, :, :]).then_inc(zh_ready, 1)

            def turn_of(b, g, turns, main, side, k=None, last=False):
                for u in range(BODY):
                    if main:
                        first, part = k == 0 and u == 0, not (last and u >= BODY - 2)
                        if first:
                            split_adj(b)
                        elif part:
                            take_part(g, u + 2)
                        if not (last and u >= BODY - 4):
                            split_x(g, u + 4, turns)
                        if first:
                            take_colsum(b)
                            take_part(g, u + 2)
                    side(u)
                    if main and part:
                        split_z(g, u + 2)

            def batch(b, main, adjacency, sums, last=False):
                a, r, g, n = b + 1, b + 2, b * T, b * TURNS
                for k in range(2):
                    turn_of(b, g + k * BODY, n + k, main, lambda u: adjacency and make(a, u + k * BODY), k)
                with act.Fori(0, LOOP_TURNS) as turn:
                    turn_of(b, g + turn * BODY + 2 * BODY, n + turn + 2, main, lambda u: adjacency and search_both(a, turn, u))
                for k in range(2):
                    turn_of(b, g + (6 + k) * BODY, n + 6 + k, main, lambda u: adjacency and mask(a, r, u + k * BODY, sums), last=last and k == 1)

            take_h(0)
            take_e(0)
            batch(-1, False, True, True)
            for u in range(4):
                split_x(0, u, 0)
            take_part(0, 0)
            split_z(0, 0)
            take_part(0, 1)
            split_z(0, 1)
            with act.Fori(0, B - 2) as b:
                batch(b, True, True, True)
            batch(B - 2, True, True, False)
            batch(B - 1, True, False, False, last=True)

        @block.gpsimd
        def _(pool):
            pool.sem_inc(row_done, ROW0)
            pool.sem_inc(sums_p, SUMS0)
            for s in range(PAIRS):
                pool.sem_inc(pair_out[s], 16)

            def clear(r):
                if not (isinstance(r, int) and r == 0):
                    pool.wait_ge(h_ps, r)
                    pool.nop(nofuse=True)
                nc.gpsimd.memset(xs_p[:, :], 0.0).then_inc(cleared_p, 1)

            def add(n, slot_half):
                pool.wait_ge(sums_p, n + SUMS0)
                nc.gpsimd.tensor_tensor(xs_p[:, :], xs_p[:, :], stage_p[:, slot_half // 2, slot_half % 2, :], ALU.add).then_inc(sums_p, 1)

            def add_time(r, turn, u):
                if u in POOL_ADDS:
                    j = POOL_ADDS[u]
                    if j == 0:
                        pool.wait_ge(cleared_p, r + 1)
                    if j % 2 == 0:
                        pool.wait_ge(staged_p[j // 2], r * (16 * (LOOP_TURNS + 1)) + turn * 16 + 16)
                    add(r * (T // 2) + turn * (2 * POOL_PAIRS) + j, j)

            def add_last(r, u):
                if u % 2 == 0:
                    fills = LOOP_TURNS + 1 if u // 2 < POOL_PAIRS else 1
                    pool.wait_ge(staged_p[u // 2], r * (16 * fills) + 16 * fills)
                add(r * (T // 2) + (T // 2 - BODY + u), u)

            def make(a, u):
                for i in at(MAKE_START, u, 3):
                    pool.wait_ge(attn_ready, a * NT + (i + 1))
                    w0 = work[:, i, 0, :]
                    nc.gpsimd.tensor_tensor(prob[:, i, :], prob[:, i, :], w0, ALU.add).then_inc(logit_sum, 1)

            def split_x(g, u):
                pool.wait_ge(xh_ready, g + (u + 1))
                nc.gpsimd.tensor_tensor(x_lo[:, u % XBUF, :], x_in[:, u // 2 % PAIRS, u % 2, :], x_hi[:, u % XBUF, :], ALU.subtract).then_inc(xl_ready, 1)

            def add_skip(g, u, turns):
                if u % 2 == 0:
                    pool.wait_ge(pair_out[u // 2], turns * 16 + 16)
                pool.wait_ge(scaled_ready, g + (u + 1 + SCALED0))
                nc.gpsimd.tensor_tensor(o_out[:, u // 2, u % 2, :], scaled[:, u % 2, :], x_in[:, u // 2, u % 2, :], ALU.add).then_inc(row_done, 1)

            def turn_of(b, g, turns, main, side, k=None, last=False):
                for u in range(BODY):
                    if main:
                        if not (last and u >= BODY - 4):
                            split_x(g, u + 4)
                        add_skip(g, u, turns)
                    side(u)

            def batch(b, main, adjacency, sums, last=False):
                a, r, g, n = b + 1, b + 2, b * T, b * TURNS
                for k in range(2):
                    turn_of(b, g + k * BODY, n + k, main, lambda u: adjacency and make(a, u + k * BODY), k)
                if sums:
                    clear(r)
                if main or sums:
                    with pool.Fori(0, LOOP_TURNS) as turn:
                        turn_of(b, g + turn * BODY + 2 * BODY, n + turn + 2, main, lambda u: sums and add_time(r, turn, u))
                for k in range(2):
                    turn_of(b, g + (6 + k) * BODY, n + 6 + k, main, lambda u: sums and k == 0 and add_last(r, u), last=last and k == 1)

            clear(0)
            with pool.Fori(0, LOOP_TURNS) as turn:
                for u in range(BODY):
                    add_time(0, turn, u)
            for u in range(BODY):
                add_last(0, u)
            batch(-1, False, True, True)
            for u in range(4):
                split_x(0, u)
            with pool.Fori(0, B - 2) as b:
                batch(b, True, True, True)
            batch(B - 2, True, True, False)
            batch(B - 1, True, False, False, last=True)

        @block.vector
        def _(dve):
            V = nc.vector
            dve.sem_inc(zsum_ready, ZSUM0)
            dve.sem_inc(zl_ready, ZL0)
            dve.sem_inc(scaled_ready, SCALED0)
            dve.sem_inc(sums_d, SUMS0)

            V.memset(chosen[:, :], 0.0).then_inc(chosen_set, 1)
            dve.wait_ge(chosen_set, 1)
            V.memset(chosen[:, :].rearrange("p (r q) -> p r q", q=Q)[:, :, 0:1], 1.0).then_inc(chosen_set, 1)
            dve.wait_ge(chosen_set, 2)
            V.tensor_copy(chosen_r[:, :], chosen[:, :]).then_inc(chosen_set, 1)
            V.memset(one[:, :], 1.0).then_inc(dve_step, 1)

            steps = [0]

            def step(instruction):
                steps[0] += 1
                instruction.then_inc(dve_step, 1)
                return steps[0]

            def after(a, n):
                dve.wait_ge(dve_step, a * STEPS + (n + 1))

            def clear(r):
                if not (isinstance(r, int) and r == 0):
                    dve.wait_ge(h_ps, r)
                V.memset(xs_d[:, :], 0.0).then_inc(cleared_d, 1)

            def add_time(r, turn, u):
                if u % 2 == 0:
                    dve.wait_ge(staged_d[u // 2], r * (16 * LOOP_TURNS) + turn * 16 + 16)
                if u == 0:
                    dve.wait_ge(cleared_d, r + 1)
                dve.wait_ge(sums_d, r * (T // 2) + turn * BODY + (u + SUMS0))
                V.tensor_tensor(xs_d[:, :], xs_d[:, :], stage_d[:, u // 2, u % 2, :], ALU.add).then_inc(sums_d, 1)

            def take_wh1(r):
                dve.wait_ge(wh_ps, r + 1)
                V.tensor_copy(wh1[:, :], ps_adj[:, 0, 0:NT]).then_inc(wh1_ready, 1)

            def score_max(a, i):
                dve.wait_ge(relu_done, a * NT + (i + 1 + RELU0))
                after(a, step(V.tensor_reduce(smax[:, i, :], work[:, i, :, :], AX.X, ALU.max)))
                V.tensor_scalar(sneg[:, i, :], smax[:, i, :], -1.0, None, ALU.mult).then_inc(smax_ready, 1)

            def attention(a, i, main):
                dve.wait_ge(exp_done, a * NT + (i + 1))
                if i == 0:
                    if main:
                        dve.wait_ge(alo_ready, a * NT)
                    dve.wait_ge(erow_ready, a + 1)
                    dve.wait_ge(wh1_ready, a + 1)
                w0, w1 = work[:, i, 0, :], work[:, i, 1, :]
                n = step(V.reciprocal(coef[:, i, :], ssum[:, i, :]))
                step(V.scalar_tensor_tensor(prob[:, i, :], e_row[:, :], wh1[:, i:i + 1], cw_sb[:, i, :], ALU.add, ALU.mult))
                after(a, n)
                after(a, step(V.tensor_tensor(coef[:, i, :], coef[:, i, :], fc_sb[:, 0:2], ALU.mult)))
                after(a, step(V.tensor_scalar(w1, w1, coef[:, i, 1:2], fc_sb[:, 2:3], ALU.mult, ALU.add)))
                after(a, step(V.scalar_tensor_tensor(w0, w0, coef[:, i, 0:1], w1, ALU.mult, ALU.add)))
                V.tensor_tensor(w0, w0, cwa_sb[:, i, :], ALU.mult).then_inc(attn_ready, 1)

            def row_max(a, i):
                dve.wait_ge(logit_sum, a * NT + (i + 1))
                after(a, step(V.tensor_reduce(lmax[:, i:i + 1], prob[:, i, :], AX.X, ALU.max)))
                V.tensor_scalar(lneg[:, i:i + 1], lmax[:, i:i + 1], -1.0, None, ALU.mult).then_inc(lneg_ready, 1)

            def normalise(a, i):
                dve.wait_ge(lexp_done, a * NT + (i + 1))
                after(a, step(V.reciprocal(lrec[:, i:i + 1], lsum[:, i:i + 1])))
                V.tensor_scalar(prob[:, i, :], prob[:, i, :], lrec[:, i:i + 1], None, ALU.mult).then_inc(prob_ready, 1)

            def make(a, u, main):
                for i in at(MAKE_START, u, 1):
                    score_max(a, i)
                for i in at(MAKE_START, u, 3):
                    attention(a, i, main)
                for i in at(MAKE_START, u, 5):
                    row_max(a, i)
                for i in at(MAKE_START, u, 7):
                    normalise(a, i)
                if u == BODY + 1:
                    start_search(a, 0)
                if u >= BODY + FIRST:
                    search(a, 0, u - BODY - FIRST)
                if u == 2 * BODY - 1:
                    start_search(a, 1)

            def start_search(a, half):
                c = slice(half * HALF, half * HALF + HALF)
                dve.wait_ge(prob_ready, a * NT + half * HALF + HALF)
                V.tensor_copy(cand[:, c], cand0_sb[:, c]).then_inc(cand_ready[half], 1)

            def search(a, half, bit):
                c = slice(half * HALF, half * HALF + HALF)
                dve.wait_ge(counted[half], a * BITS + bit + 1)
                V.tensor_scalar(miss[:, c], count[:, c], float(ENOUGH), bitf_sb[:, bass.ds(bit, 1)], ALU.is_lt, ALU.mult).then_inc(missed[half], 1)
                dve.wait_ge(missed[half], a * BITS + bit + 1)
                V.scalar_tensor_tensor(cand[:, c], miss[:, c], biti_sb[:, bass.ds(bit + 1, 1)], cand[:, c], ALU.bitwise_xor, ALU.bitwise_xor).then_inc(cand_ready[half], 1)

            def search_both(a, turn, u):
                for half, tile, n in COUNTS[u % 4]:
                    if tile == HALF - 1:
                        search(a, half, turn * SEARCHES + (u // 4 * 3 + n + (SEARCHES if half == 0 else 0)))

            def mask(a, r, u, sums):
                for half in range(2):
                    if u == MASK_START[half * HALF]:
                        c = slice(half * HALF, half * HALF + HALF)
                        dve.wait_ge(cand_ready[half], a * (BITS + 1) + (BITS + 1))
                        after(a, step(V.tensor_scalar(thr[:, c], cand[:, c].bitcast(F32), -1.0, None, ALU.mult)))
                for i in at(MASK_START, u, 0):
                    p, w = prob[:, i, :], work[:, i, 0, :]
                    after(a, step(V.scalar_tensor_tensor(w, p, thr[:, i:i + 1], p, ALU.is_lt, ALU.add)))
                    after(a, step(V.tensor_reduce(kth[:, i:i + 1], w, AX.X, ALU.min)))
                    V.tensor_scalar(kth_neg[:, i:i + 1], kth[:, i:i + 1], -1.0, None, ALU.mult).then_inc(kth_ready, 1)
                for i in at(MASK_START, u, 2):
                    w, squares = work[:, i, 0, :], work[:, i, 1, :]
                    dve.wait_ge(balanced, a * NT + (i + 1))
                    step(V.tensor_tensor_scan(w, squares, one[:, 0:1].to_broadcast([P, N]), 0.0, ALU.add, ALU.subtract))
                    after(a, step(V.tensor_tensor(ties_neg[:, i:i + 1], balance[:, i:i + 1], unequal[:, i:i + 1], ALU.add)))
                    step(V.tensor_scalar(ties_neg[:, i:i + 1], ties_neg[:, i:i + 1], 0.5, -float(KEEP), ALU.mult, ALU.add))
                for i in at(MASK_START, u, 3):
                    p, w = prob[:, i, :], work[:, i, 0, :]
                    after(a, steps[0])
                    after(a, step(V.scalar_tensor_tensor(w, sign[:, i, :], BIG, w, ALU.mult, ALU.add)))
                    V.scalar_tensor_tensor(p, w, ties_neg[:, i:i + 1], p, ALU.is_ge, ALU.mult).then_inc(masked, 1)
                if FIRST <= u < BODY:
                    search(a, 1, BITS - SEARCHES + u - FIRST)
                if sums and u == PROJECT_WH + 1:
                    take_wh1(r)

            def split_adj(b):
                for i in range(NT):
                    dve.wait_ge(ahi_ready, b * NT + (i + 1))
                    V.tensor_tensor(adj_lo[:, i, :], prob[:, i, :], adj_hi[:, i, :], ALU.subtract).then_inc(alo_ready, 1)

            def split_colsum(b):
                dve.wait_ge(colsum_hi, b + 1)
                low = slice(Q, 2 * Q)
                V.tensor_tensor(colsum[low, :], ps_adj[low, 1, :], colsum[low, :], ALU.subtract).then_inc(colsum_split, 1)

            def sum_z(g, u):
                v = ps_mix[u % 2][:, :].rearrange("p (i s d) -> p i s d", i=NT, s=2)
                dve.wait_ge(part_ready, g + (u + 1))
                dve.wait_ge(zl_ready, g + (u + ZL0))
                V.tensor_tensor(zsum[:, :, :], v[:, :, 0, :], zpart[:, :, :], ALU.add).then_inc(zsum_ready, 1)

            def split_z(g, u):
                dve.wait_ge(zh_ready, g + (u + 1))
                V.tensor_tensor(z_lo[:, u % ZBUF, :, :], zsum[:, :, :], z_hi[:, u % ZBUF, :, :], ALU.subtract).then_inc(zl_ready, 1)

            def scale_out(g, u):
                dve.wait_ge(node_done, g + (u + 1 + NODE0))
                dve.wait_ge(row_done, g + (u - 1 + ROW0))
                V.scalar_tensor_tensor(scaled[:, u % 2, :], ps_out[u % 2][:, :], cb_sb[:, 0:1], emb_sb[:, :], ALU.add, ALU.mult).then_inc(scaled_ready, 1)

            def turn_of(b, g, main, side, k=None, last=False):
                for u in range(BODY):
                    z = main and not (last and u >= BODY - 2)
                    if main and k == 0 and u == 0:
                        split_colsum(b)
                    if z:
                        sum_z(g, u + 2)
                    side(u)
                    if z:
                        split_z(g, u + 2)
                    if main and k == 7 and u == BODY - 1 and not last:
                        split_adj(b + 1)
                    if main:
                        scale_out(g, u)

            def batch(b, main, adjacency, sums, last=False):
                a, r, g = b + 1, b + 2, b * T
                steps[0] = 0
                for k in range(2):
                    turn_of(b, g + k * BODY, main, lambda u: adjacency and make(a, u + k * BODY, main), k)
                if sums:
                    clear(r)
                with dve.Fori(0, LOOP_TURNS) as turn:
                    def side(u):
                        if sums:
                            add_time(r, turn, u)
                        if adjacency:
                            search_both(a, turn, u)
                    turn_of(b, g + turn * BODY + 2 * BODY, main, side)
                for k in range(2):
                    turn_of(b, g + (6 + k) * BODY, main, lambda u: adjacency and mask(a, r, u + k * BODY, sums), 6 + k, last=last and k == 1)
                assert steps[0] == (STEPS if adjacency else 0), steps

            clear(0)
            with dve.Fori(0, LOOP_TURNS) as turn:
                for u in range(BODY):
                    add_time(0, turn, u)
            dve.wait_ge(pre_sb, 5)
            V.tensor_tensor(p_split[:, 1, :], pT[:, :], p_split[:, 0, :], ALU.subtract).then_inc(pre_sb, 1)
            low = slice(2 * Q, 3 * Q)
            V.tensor_tensor(pb_parts[low, :], pb_row[low, :], pb_parts[low, :], ALU.subtract).then_inc(pre_sb, 1)
            take_wh1(0)
            batch(-1, False, True, True)
            for u in range(2):
                sum_z(0, u)
                split_z(0, u)
            split_adj(0)
            with dve.Fori(0, B - 2) as b:
                batch(b, True, True, True)
            batch(B - 2, True, True, False)
            batch(B - 1, True, False, False, last=True)


def kernel(**inputs):
    from concourse import bacc
    from concourse.bass_utils import run_bass_kernel_spmd

    v = {k: np.asarray(w) for k, w in inputs.items()}
    t = lambda m: np.ascontiguousarray(m.T)
    pow2 = np.append(2.0 ** np.arange(BITS - 1, -1, -1), 0.0)
    data = [
        ("x", v["x"].transpose(0, 3, 1, 2).reshape(B, T // 2, 2, C, N).transpose(0, 1, 3, 2, 4)),
        ("w_nat", v["L0_conv_W_w"]),
        ("w_t", t(v["L0_conv_W_w"])),
        ("w_b", v["L0_conv_W_b"].reshape(C, 1)),
        ("theta_t", t(v["L0_conv_theta"])),
        ("conv_t", t(v["L0_conv_conv_w"])),
        ("conv_b", v["L0_conv_conv_b"].reshape(C, 1)),
        ("mem_t", t(v["L0_conv_memory"])),
        ("a_vec", t(v["L0_conv_a_vec"].reshape(2, C))),
        ("cw", v["L0_conv_cw"]),
        ("cwa", v["L0_conv_cwa"]),
        ("fc", np.concatenate([v["L0_conv_fc_w"].reshape(1, 2), v["L0_conv_fc_b"].reshape(1, 1)], axis=1)),
        ("emb", v["L0_conv_emb"].reshape(C, N)),
        ("bits_f", np.tile(pow2.astype(np.float32), (P, 1))),
        ("bits_i", np.tile(pow2.astype(np.int32), (P, 1))),
        ("cand0", np.full((P, NT), -2 ** 31 + 2 ** (BITS - 1), np.int32)),
    ]
    nc = bacc.Bacc("TRN2", target_bir_lowering=False, num_devices=1)
    arrays, args = {}, []
    for name, w in data:
        w = np.ascontiguousarray(w)
        arrays[name + "_dram"] = w
        args.append(nc.dram_tensor(name + "_dram", w.shape, mybir.dt.from_np(w.dtype), kind="ExternalInput").ap())
    out = nc.dram_tensor("out_dram", (B, T // 2, C, 2, N), F32, kind="ExternalOutput").ap()
    build(nc, *args, out)
    r = run_bass_kernel_spmd(nc, [arrays], core_ids=[0])
    o = r.results[0]["out_dram"]
    return np.ascontiguousarray(o.transpose(0, 2, 4, 1, 3).reshape(B, C, N, T))
```
